# Optimizing a Trainium2 kernel written in Bass

```python
import numpy as np
import jax
import jax.numpy as jnp

def _softmax(x, axis=-1):
    return jax.nn.softmax(x, axis=axis)

def _gelu(x):
    return jax.nn.gelu(x, approximate=True)

def _silu(x):
    return jax.nn.silu(x)

def _sigmoid(x):
    return jax.nn.sigmoid(x)

def _layernorm(x, axis=-1, eps=1e-05):
    m = jnp.mean(x, axis=axis, keepdims=True)
    v = jnp.var(x, axis=axis, keepdims=True)
    return (x - m) / jnp.sqrt(v + eps)

def _scatter_add(tgt, idx, src, axis=0):
    return tgt.at[idx].add(src)

def _segment_sum(src, seg, n):
    return jax.ops.segment_sum(src, seg, n)
kernel_name = 'mk_conv_seq_d1_conv_nchw512_r4_7d25ea'

def setup_inputs(seed: int=0):
    np.random.seed(seed)
    _w = jnp.asarray

    def _rec_inputs():
        import jax
        import jax.numpy as jnp
        _gk = jax.random.key(seed)
        x = -0.0002928 + 1 * jax.random.normal(jax.random.fold_in(_gk, 1), (2, 128, 16, 16), jnp.float32)
        return x
    x = _rec_inputs()

    def _L0_conv_setup():
        import jax, jax.numpy as jnp
        import numpy as np
        C = 128
        NUM_HEADS = 8

        def _attention(x, Wq, bq, Wk, bk, Wv, bv, gamma):
            B, Cc, H, W = x.shape
            h = NUM_HEADS
            d = Cc // h
            N = H * W
            xf = x.reshape(B, Cc, N)
            q = jnp.einsum('oc,bcn->bon', Wq, xf) + bq[None, :, None]
            k = jnp.einsum('oc,bcn->bon', Wk, xf) + bk[None, :, None]
            v = jnp.einsum('oc,bcn->bon', Wv, xf) + bv[None, :, None]
            q = q.reshape(B, h, d, N)
            k = k.reshape(B, h, d, N)
            v = v.reshape(B, h, d, N)
            energy = jnp.einsum('bhdi,bhdj->bhij', q, k)
            attn = jax.nn.softmax(energy, axis=-1)
            out = jnp.einsum('bhij,bhdj->bhdi', attn, v)
            out = out.reshape(B, Cc, H, W)
            return gamma[0] * out + x
        key = jax.random.key(seed)
        ks = jax.random.split(key, 7)
        B, H, W = (2, 16, 16)
        s = 1.0 / np.sqrt(C)
        x = jax.random.normal(ks[0], (B, C, H, W), dtype=jnp.float32)
        Wq = jax.random.normal(ks[1], (C, C), dtype=jnp.float32) * s
        bq = jnp.zeros((C,), dtype=jnp.float32)
        Wk = jax.random.normal(ks[2], (C, C), dtype=jnp.float32) * s
        bk = jnp.zeros((C,), dtype=jnp.float32)
        Wv = jax.random.normal(ks[3], (C, C), dtype=jnp.float32) * s
        bv = jnp.zeros((C,), dtype=jnp.float32)
        gamma = jnp.array([0.5], dtype=jnp.float32)
        return {'x': x, 'Wq': Wq, 'bq': bq, 'Wk': Wk, 'bk': bk, 'Wv': Wv, 'bv': bv, 'gamma': gamma}
    _L0_conv_all = _L0_conv_setup()
    _L0_conv_in = {k: v for k, v in _L0_conv_all.items() if k in ('Wq', 'bq', 'Wk', 'bk', 'Wv', 'bv', 'gamma')}
    del _L0_conv_all
    return {'x': x, 'L0_conv_Wq': _L0_conv_in['Wq'], 'L0_conv_bq': _L0_conv_in['bq'], 'L0_conv_Wk': _L0_conv_in['Wk'], 'L0_conv_bk': _L0_conv_in['bk'], 'L0_conv_Wv': _L0_conv_in['Wv'], 'L0_conv_bv': _L0_conv_in['bv'], 'L0_conv_gamma': _L0_conv_in['gamma']}

def reference(x, L0_conv_Wq, L0_conv_bq, L0_conv_Wk, L0_conv_bk, L0_conv_Wv, L0_conv_bv, L0_conv_gamma):
    import jax
    import jax.numpy as jnp

    def _L0_conv_ref(x, Wq, bq, Wk, bk, Wv, bv, gamma):
        import jax, jax.numpy as jnp
        import numpy as np
        C = 128
        NUM_HEADS = 8

        def _attention(x, Wq, bq, Wk, bk, Wv, bv, gamma):
            B, Cc, H, W = x.shape
            h = NUM_HEADS
            d = Cc // h
            N = H * W
            xf = x.reshape(B, Cc, N)
            q = jnp.einsum('oc,bcn->bon', Wq, xf) + bq[None, :, None]
            k = jnp.einsum('oc,bcn->bon', Wk, xf) + bk[None, :, None]
            v = jnp.einsum('oc,bcn->bon', Wv, xf) + bv[None, :, None]
            q = q.reshape(B, h, d, N)
            k = k.reshape(B, h, d, N)
            v = v.reshape(B, h, d, N)
            energy = jnp.einsum('bhdi,bhdj->bhij', q, k)
            attn = jax.nn.softmax(energy, axis=-1)
            out = jnp.einsum('bhij,bhdj->bhdi', attn, v)
            out = out.reshape(B, Cc, H, W)
            return gamma[0] * out + x
        return _attention(x, Wq, bq, Wk, bk, Wv, bv, gamma)

    def _gn(v, G=32, eps=1e-05):
        B_, C_, H_, W_ = v.shape
        g = v.reshape(B_, G, C_ // G, H_, W_)
        m = jnp.mean(g, axis=(2, 3, 4), keepdims=True)
        s = jnp.var(g, axis=(2, 3, 4), keepdims=True)
        return ((g - m) / jnp.sqrt(s + eps)).reshape(v.shape)

    def _ln_c(v, eps=1e-06):
        m = jnp.mean(v, axis=1, keepdims=True)
        s = jnp.var(v, axis=1, keepdims=True)
        return (v - m) / jnp.sqrt(s + eps)

    def _ln_t(v, eps=1e-05):
        m = jnp.mean(v, axis=-1, keepdims=True)
        s = jnp.var(v, axis=-1, keepdims=True)
        return (v - m) / jnp.sqrt(s + eps)

    def _to_tokens(v):
        B_, C_, H_, W_ = v.shape
        return v.reshape(B_, C_, H_ * W_).transpose(0, 2, 1)

    def _from_tokens(t, like):
        B_, C_, H_, W_ = like.shape
        return t.transpose(0, 2, 1).reshape(B_, C_, H_, W_)
    x = _L0_conv_ref(x, L0_conv_Wq, L0_conv_bq, L0_conv_Wk, L0_conv_bk, L0_conv_Wv, L0_conv_bv, L0_conv_gamma)
    return x

_drawn_inputs = setup_inputs


def setup_inputs(seed=0):
    import zlib

    import numpy as np

    out = dict(_drawn_inputs(seed))
    spreads = {'L0_conv_bq': (0.0, 0.1), 'L0_conv_bk': (0.0, 0.1), 'L0_conv_bv': (0.0, 0.1)}
    factors = {}
    for name, (base, spread) in spreads.items():
        noise = np.random.default_rng([zlib.crc32(name.encode()), seed]).standard_normal(out[name].shape)
        drawn = base * np.exp(spread * noise) if base else spread * noise
        out[name] = jnp.asarray(drawn.astype(out[name].dtype))
    for name, factor in factors.items():
        out[name] = (out[name] * factor).astype(out[name].dtype)
    return out
```

```python
import concourse.bass as bass
from concourse import mybir
from contextlib import ExitStack

B, C, HW = 2, 128, 256
HEADS, D = 8, 16
Q = 32
HPC = 128 // Q
GROUPS = HEADS // HPC
CHUNKS = B * GROUPS
T = HW // 128
PAIR = 2
WARM = 6

BQ, BK, BK_LO, BK_H1, IS_LO, IS_HI, BV, GAMMA = 0, 2, 4, 6, 8, 9, 10, 11
PARAMS = 12


def build(nc, x, wqk, par, wv, ident, out):
    f32, f32r, bf16 = mybir.dt.float32, mybir.dt.float32r, mybir.dt.bfloat16
    ACT, ALU, AX = mybir.ActivationFunctionType, mybir.AluOpType, mybir.AxisListType
    IDENT = ACT.Identity

    with ExitStack() as ctx:
        def sb(name, shape, dt=f32):
            return ctx.enter_context(nc.sbuf_tensor(name, shape, dt))

        def ps(name, shape):
            return ctx.enter_context(nc.psum_tensor(name, shape, f32))

        def sem(name):
            return ctx.enter_context(nc.semaphore(name))

        x_sb = sb("x_sb", [C, B, HW])
        wqk_sb = sb("wqk_sb", [C, GROUPS, 2, 128])
        wv_sb = sb("wv_sb", [C, C])
        par_sb = sb("par_sb", [128, PARAMS])
        id_sb = sb("id_sb", [128, 128])
        id_r = sb("id_r", [128, 128], f32r)
        junk = sb("junk", [128, Q], bf16)
        q_hh = sb("q_hh", [128, CHUNKS, HW], f32r)
        q_lo = sb("q_lo", [128, CHUNKS, HW], f32r)
        q_ls = sb("q_ls", [128, CHUNKS, HW], f32r)
        k_tmp = sb("k_tmp", [128, CHUNKS, HW], f32r)
        k_hl = sb("k_hl", [128, CHUNKS, HW], f32r)
        k_h1 = sb("k_h1", [128, CHUNKS, HW], f32r)
        v_sb = sb("v_sb", [128, B * T, HEADS, 2 * D])
        rowmax = sb("rowmax", [128, CHUNKS, HPC, T])
        shift = sb("shift", [128, CHUNKS, T, HPC, Q], f32r)
        p_sb = sb("p_sb", [128, 2, HPC, T, HW])
        o_sb = sb("o_sb", [128, CHUNKS, HW])
        rden = sb("rden", [128, CHUNKS, T, HPC])
        o_t = sb("o_t", [128, B, T, HEADS, D])
        gbv = sb("gbv", [128, 1])
        xg = sb("xg", [C, B, HW])
        y_sb = sb("y_sb", [C, B, HW])

        s_ps = ps("s_ps", [128, 2, PAIR, T, HW])
        banks = [ps(f"bank{n}", [128, 512]) for n in range(4, 8)]
        e_ps = banks[0:2]
        m_ps, o_ps = banks[2], banks[3]
        q_ps = [banks[2 * (c % 2)][:, 0:HW] for c in range(CHUNKS)]
        k_ps = [banks[2 * (c % 2) + 1][:, 0:HW] for c in range(CHUNKS)]
        v_ps = banks[0]

        in_w0, in_x0, in_w1, in_x1, in_wv, in_id, in_par = (
            sem(n) for n in ("in_w0", "in_x0", "in_w1", "in_x1", "in_wv", "in_id", "in_par"))
        junk_set, ones_set, shift_zeroed, id_rounded = (
            sem(n) for n in ("junk_set", "ones_set", "shift_zeroed", "id_rounded"))
        q_projected, k_projected, v_projected = (sem(n) for n in ("q_projected", "k_projected", "v_projected"))
        q_hh_ready, q_lo_ready, q_ls_ready = (sem(n) for n in ("q_hh_ready", "q_lo_ready", "q_ls_ready"))
        k_tmp_ready, k_hl_ready, k_h1_ready = (sem(n) for n in ("k_tmp_ready", "k_hl_ready", "k_h1_ready"))
        v_ready, gbv_ready, xg_ready = (sem(n) for n in ("v_ready", "gbv_ready", "xg_ready"))
        pair_scored, pair_maxed, shift_ready, shift_placed = (
            sem(n) for n in ("pair_scored", "pair_maxed", "shift_ready", "shift_placed"))
        head_scored, head_exped, chunk_summed, sums_copied = (
            sem(n) for n in ("head_scored", "head_exped", "chunk_summed", "sums_copied"))
        sums_turned, rden_ready, o_t_ready, image_turned, y_ready = (
            sem(n) for n in ("sums_turned", "rden_ready", "o_t_ready", "image_turned", "y_ready"))
        stored = [sem(f"stored{b}") for b in range(B)]

        def rows(g):
            return slice(Q * g, Q * g + Q)

        x_d = x.rearrange("b c h w -> b c (h w)")
        out_d = out.rearrange("b c h w -> b c (h w)")
        block = ctx.enter_context(nc.Block())

        @block.sync
        def _(sp):
            sp.dma_start(wqk_sb[:, 0], wqk[:, 0]).then_inc(in_w0, 16)
            sp.dma_start(par_sb[:], par).then_inc(in_par, 16)
            sp.dma_start(wqk_sb[:, 1], wqk[:, 1]).then_inc(in_w1, 16)
            sp.dma_start(id_sb[:], ident).then_inc(in_id, 16)
            for b in range(B):
                sp.wait_ge(y_ready, b + 1)
                sp.dma_start(out_d[b], y_sb[:, b]).then_inc(stored[b], 16)
            for b in range(B):
                sp.wait_ge(stored[b], 16)

        @block.gpsimd
        def _(pool):
            nc.gpsimd.memset(shift[:].bitcast(f32), 0.0).then_inc(shift_zeroed, 1)
            nc.gpsimd.memset(v_sb[:, :, :, D:2 * D], 1.0).then_inc(ones_set, 1)
            pool.wait_ge(in_id, 16)
            nc.gpsimd.tensor_copy(id_r[:], id_sb[:]).then_inc(id_rounded, 1)
            pool.wait_ge(in_par, 16)
            nc.gpsimd.tensor_tensor(gbv[:], par_sb[:, BV:BV + 1], par_sb[:, GAMMA:GAMMA + 1],
                                    ALU.mult).then_inc(gbv_ready, 1)
            pool.wait_ge(shift_zeroed, 1)

            def negate(c):
                pool.wait_ge(pair_maxed, 2 * c + 2)
                nc.gpsimd.tensor_scalar(shift[:, c, :, :, D:D + 1],
                                        rowmax[:, c].rearrange("p g (t o) -> p t g o", o=1), -1.0, None,
                                        ALU.mult).then_inc(shift_ready, 1)

            negate(0)
            pool.wait_ge(gbv_ready, 1)
            pool.wait_ge(in_x0, 16)
            pool.wait_ge(in_x1, 16)
            for b in range(B):
                nc.gpsimd.tensor_scalar(xg[:, b], x_sb[:, b], gbv[:], 0.0, ALU.add,
                                        ALU.add).then_inc(xg_ready, 1)
                negate(b + 1)
            negate(3)

        @block.scalar
        def _(act):
            act.dma_start(x_sb[:, 0], x_d[0]).then_inc(in_x0, 16)
            act.dma_start(x_sb[:, 1], x_d[1]).then_inc(in_x1, 16)
            act.dma_start(wv_sb[:], wv).then_inc(in_wv, 16)
            act.wait_ge(in_par, 16)

            def col(n):
                return par_sb[:, n:n + 1]

            def split(c):
                g = c % GROUPS
                act.wait_ge(q_projected, c + 1)
                nc.scalar.activation(q_hh[:, c], q_ps[c], IDENT, bias=col(BQ + g)).then_inc(q_hh_ready, 1)
                act.wait_ge(k_projected, c + 1)
                nc.scalar.activation(k_tmp[:, c], k_ps[c], IDENT, bias=col(BK_LO + g),
                                     scale=col(IS_LO)).then_inc(k_tmp_ready, 1)

            def split_h1(c):
                act.wait_ge(k_hl_ready, c + 1)
                nc.scalar.activation(k_h1[:, c], k_ps[c], IDENT, bias=col(BK_H1 + c % GROUPS),
                                     scale=col(IS_HI)).then_inc(k_h1_ready, 1)

            def exp(c, g):
                n = HPC * c + g
                act.wait_ge(head_scored, n + 1)
                if c >= 2:
                    act.wait_ge(chunk_summed, c - 1)
                nc.scalar.activation(p_sb[:, c % 2, g].rearrange("p t n -> p (t n)"), e_ps[n % 2][:],
                                     ACT.Exp).then_inc(head_exped, 1)

            def copy_sums(c):
                act.wait_ge(chunk_summed, c + 1)
                nc.scalar.activation(o_sb[:, c], o_ps[:, 0:HW], ACT.Copy).then_inc(sums_copied, 1)

            split(0)
            split_h1(0)
            split(1)
            split_h1(1)
            split(2)
            split_h1(2)
            split(3)
            split_h1(3)
            act.wait_ge(v_projected, 1)
            act.wait_ge(ones_set, 1)
            nc.scalar.activation(v_sb[:, :, :, 0:D].rearrange("p t h d -> p (t h) d"),
                                 v_ps[:].rearrange("p (n d) -> p n d", d=D), ACT.Copy).then_inc(v_ready, 1)
            for c in range(CHUNKS):
                exp(c, 0)
                exp(c, 1)
                if c:
                    copy_sums(c - 1)
                exp(c, 2)
                exp(c, 3)
            copy_sums(CHUNKS - 1)

        @block.vector
        def _(dve):
            nc.vector.memset(junk[:], 0.5).then_inc(junk_set, 1)
            dve.wait_ge(in_par, 16)

            def col(n):
                return par_sb[:, n:n + 1]

            def split(c):
                g = c % GROUPS
                dve.wait_ge(k_tmp_ready, c + 1)
                nc.vector.scalar_tensor_tensor(out=k_hl[:, c], in0=k_ps[c], scalar=col(BK + g),
                                               in1=k_tmp[:, c].bitcast(f32), op0=ALU.add,
                                               op1=ALU.subtract).then_inc(k_hl_ready, 1)
                dve.wait_ge(q_hh_ready, c + 1)
                nc.vector.scalar_tensor_tensor(out=q_lo[:, c], in0=q_ps[c], scalar=col(BQ + g),
                                               in1=q_hh[:, c].bitcast(f32), op0=ALU.add,
                                               op1=ALU.subtract).then_inc(q_lo_ready, 1)

            def maximum(c, p):
                n = 2 * c + p
                dve.wait_ge(pair_scored, n + 1)
                nc.vector.tensor_reduce(rowmax[:, c, PAIR * p:PAIR * p + PAIR], s_ps[:, n % 2],
                                        axis=AX.X, op=ALU.max).then_inc(pair_maxed, 1)

            def place(c):
                dve.wait_ge(shift_placed, c + 1)
                dve.wait_ge(q_lo_ready, c + 1)
                nc.vector.scalar_tensor_tensor(out=q_ls[:, c], in0=q_lo[:, c].bitcast(f32), scalar=col(IS_HI),
                                               in1=m_ps[:, 0:HW], op0=ALU.mult,
                                               op1=ALU.add).then_inc(q_ls_ready, 1)

            def normalise(c):
                b, g = c // GROUPS, c % GROUPS
                sums = m_ps[:, HW:2 * HW].rearrange("p (t g d) -> p t g d", t=T, d=Q)
                dve.wait_ge(sums_turned, c + 1)
                nc.vector.reciprocal(rden[:, c], sums[:, :, :, D]).then_inc(rden_ready, 1)
                dve.wait_ge(rden_ready, c + 1)
                for t in range(T):
                    last = nc.vector.tensor_tensor(o_t[:, b, t, HPC * g:HPC * g + HPC], sums[:, t, :, 0:D],
                                            rden[:, c, t].rearrange("p (g o) -> p g o", o=1).to_broadcast([128, HPC, D]), ALU.mult)
                last.then_inc(o_t_ready, 1)

            def residual(b):
                dve.wait_ge(image_turned, b + 1)
                dve.wait_ge(xg_ready, b + 1)
                nc.vector.scalar_tensor_tensor(out=y_sb[:, b], in0=o_ps[:, HW:2 * HW], scalar=col(GAMMA),
                                               in1=xg[:, b], op0=ALU.mult, op1=ALU.add).then_inc(y_ready, 1)

            split(0)
            split(1)
            maximum(0, 0)
            split(2)
            maximum(0, 1)
            split(3)
            maximum(1, 0)
            place(0)
            maximum(1, 1)
            for c in range(1, CHUNKS):
                place(c)
                if c + 1 < CHUNKS:
                    maximum(c + 1, 0)
                    maximum(c + 1, 1)
                if c >= 2:
                    normalise(c - 2)
            residual(0)
            normalise(CHUNKS - 2)
            normalise(CHUNKS - 1)
            residual(B - 1)

        @block.tensor
        def _(pe):
            def mm(o, lhsT, rhs, start=True, stop=True):
                return nc.tensor.matmul(o, lhsT, rhs, start=start, stop=stop)

            def project(c):
                b, g = c // GROUPS, c % GROUPS
                if c >= 2:
                    pe.wait_ge(q_hh_ready, c - 1)
                    pe.wait_ge(q_lo_ready, c - 1)
                mm(q_ps[c], wqk_sb[:, g, 0], x_sb[:, b]).then_inc(q_projected, 1)
                if c >= 2:
                    pe.wait_ge(k_h1_ready, c - 1)
                mm(k_ps[c], wqk_sb[:, g, 1], x_sb[:, b]).then_inc(k_projected, 1)

            def score(c, p):
                n = 2 * c + p
                if n >= 2:
                    pe.wait_ge(pair_maxed, n - 1)
                pe.wait_ge(q_hh_ready, c + 1)
                pe.wait_ge(k_hl_ready, c + 1)
                for i in range(PAIR):
                    g = PAIR * p + i
                    for t in range(T):
                        last = mm(s_ps[:, n % 2, i, t], q_hh[rows(g), c, 128 * t:128 * t + 128],
                                  k_hl[rows(g), c])
                last.then_inc(pair_scored, 1)

            def turn_shift(c):
                pe.wait_ge(shift_ready, c + 1)
                if c:
                    pe.wait_ge(q_ls_ready, c)
                if c >= 3:
                    pe.wait_ge(o_t_ready, c - 2)
                for t in range(T):
                    last = mm(m_ps[:, 128 * t:128 * t + 128], shift[:, c, t].rearrange("p g r -> p (g r)"),
                              id_r[:])
                last.then_inc(shift_placed, 1)

            def score_shifted(c, g):
                n = HPC * c + g
                if g == 0:
                    pe.wait_ge(q_ls_ready, c + 1)
                if n >= 2:
                    pe.wait_ge(head_exped, n - 1)
                for t in range(T):
                    o = e_ps[n % 2][:, HW * t:HW * t + HW]
                    keys = slice(128 * t, 128 * t + 128)
                    mm(o, k_hl[rows(g), c, keys], q_hh[rows(g), c], stop=False)
                    last = mm(o, k_h1[rows(g), c, keys], q_ls[rows(g), c], start=False)
                last.then_inc(head_scored, 1)

            def weigh(c):
                b, group = c // GROUPS, c % GROUPS
                pe.wait_ge(head_exped, HPC * c + HPC)
                pe.wait_ge(v_ready, 1)
                if c:
                    pe.wait_ge(sums_copied, c)
                if c == GROUPS + 1:
                    pe.wait_ge(y_ready, 1)
                for t in range(T):
                    for g in range(HPC):
                        last = mm(o_ps[rows(g), 0:HW], v_sb[:, T * b + t, HPC * group + g],
                                  p_sb[:, c % 2, g, t], start=(t == 0), stop=(t == T - 1))
                last.then_inc(chunk_summed, 1)

            def turn_sums(c):
                pe.wait_ge(sums_copied, c + 1)
                if c:
                    pe.wait_ge(o_t_ready, c)
                pe.wait_ge(q_ls_ready, min(c + 3, CHUNKS))
                for t in range(T):
                    last = nc.tensor.transpose(m_ps[:, HW + 128 * t:HW + 128 * t + 128],
                                               o_sb[:, c, 128 * t:128 * t + 128], id_sb[:])
                last.then_inc(sums_turned, 1)

            def turn_image(b):
                pe.wait_ge(o_t_ready, GROUPS * (b + 1))
                pe.wait_ge(sums_copied, GROUPS * (b + 1) + (b + 1 < B))
                for t in range(T):
                    last = nc.tensor.transpose(o_ps[:, HW + 128 * t:HW + 128 * t + 128],
                                               o_t[:, b, t].rearrange("p h d -> p (h d)"), id_sb[:])
                last.then_inc(image_turned, 1)

            pe.wait_ge(junk_set, 1)
            for n in range(WARM):
                mm(s_ps[0:Q, 0, 0].rearrange("p t n -> p (t n)"), junk[:], junk[:, 0:1].to_broadcast([128, 512]))
            pe.wait_ge(in_w0, 16)
            pe.wait_ge(in_x0, 16)
            project(0)
            pe.wait_ge(in_w1, 16)
            project(1)
            score(0, 0)
            score(0, 1)
            pe.wait_ge(in_x1, 16)
            project(2)
            score(1, 0)
            project(3)
            pe.wait_ge(in_wv, 16)
            pe.wait_ge(q_hh_ready, 3)
            pe.wait_ge(q_lo_ready, 3)
            for n in range(B * T):
                last = mm(v_ps[:, 128 * n:128 * n + 128], x_sb[:, n // T, 128 * (n % T):128 * (n % T) + 128],
                          wv_sb[:])
            last.then_inc(v_projected, 1)
            pe.wait_ge(id_rounded, 1)
            pe.wait_ge(q_hh_ready, 4)
            pe.wait_ge(q_lo_ready, 4)
            turn_shift(0)
            score(1, 1)
            pe.wait_ge(v_ready, 1)
            pe.wait_ge(k_h1_ready, 3)
            for c in range(CHUNKS):
                score_shifted(c, 0)
                score_shifted(c, 1)
                if c + 2 < CHUNKS:
                    score(c + 2, 0)
                score_shifted(c, 2)
                if c == 0:
                    pe.wait_ge(k_h1_ready, 4)
                if c + 1 < CHUNKS:
                    turn_shift(c + 1)
                if c == GROUPS + 1:
                    turn_image(0)
                score_shifted(c, 3)
                if c + 2 < CHUNKS:
                    score(c + 2, 1)
                weigh(c)
                if c:
                    turn_sums(c - 1)
            turn_sums(CHUNKS - 1)
            turn_image(B - 1)


def kernel(x, L0_conv_Wq, L0_conv_bq, L0_conv_Wk, L0_conv_bk, L0_conv_Wv, L0_conv_bv, L0_conv_gamma):
    import numpy as np
    import concourse.bacc as bacc
    from concourse.bass_utils import run_bass_kernel_spmd

    def twice(a):
        a = np.asarray(a)
        a = a.reshape(a.shape[:-1] + (GROUPS, HPC, 1, D))
        return np.ascontiguousarray(np.broadcast_to(a, a.shape[:-2] + (2, D))).reshape(a.shape[:-4] + (GROUPS, 128))

    wq_t = twice(np.asarray(L0_conv_Wq).T)
    wk_t = twice(np.asarray(L0_conv_Wk).T)
    wqk = np.ascontiguousarray(np.stack([wq_t, wk_t], axis=2))
    upper = (np.arange(128) % Q) < D
    par = np.zeros((128, PARAMS), np.float32)
    for g in range(GROUPS):
        par[:, BQ + g] = twice(L0_conv_bq)[g]
        par[:, BK + g] = twice(L0_conv_bk)[g]
        par[~upper, BK_LO + g] = twice(L0_conv_bk)[g][~upper]
        par[upper, BK_H1 + g] = twice(L0_conv_bk)[g][upper]
        par[~upper, BK_H1 + g] = 1.0
    par[~upper, IS_LO] = 1.0
    par[upper, IS_HI] = 1.0
    par[:, BV] = np.asarray(L0_conv_bv)
    par[:, GAMMA] = np.asarray(L0_conv_gamma)[0]
    arrays = {
        "x_dram": np.ascontiguousarray(x),
        "wqk_dram": wqk,
        "par_dram": par,
        "wv_dram": np.ascontiguousarray(np.asarray(L0_conv_Wv).T),
        "ident_dram": np.eye(128, dtype=np.float32),
    }
    nc = bacc.Bacc("TRN2", target_bir_lowering=False, num_devices=1)
    f32 = mybir.dt.float32
    args = [nc.dram_tensor(n, a.shape, f32, kind="ExternalInput").ap() for n, a in arrays.items()]
    out = nc.dram_tensor("out_dram", (B, C, 16, 16), f32, kind="ExternalOutput").ap()
    build(nc, *args, out)
    return run_bass_kernel_spmd(nc, [arrays], core_ids=[0]).results[0]["out_dram"]
```

```python
import concourse.bass as bass
from concourse import mybir
from contextlib import ExitStack

B, C, HW = 2, 128, 256
HEADS, D = 8, 16
Q = 32
HPC = 128 // Q
AHEAD = 6
GROUPS = HEADS // HPC
CHUNKS = B * GROUPS
NH = HPC * CHUNKS
T = HW // 128
SLOTS = 3
WARM = 6

BQ, BK, BK_LO, BK_H1, IS_LO, IS_HI, BV, GAMMA, HEAD = 0, 2, 4, 6, 8, 9, 10, 11, 12
PARAMS = 16


def build(nc, first, second, third, out):
    f32, f32r, bf16 = mybir.dt.float32, mybir.dt.float32r, mybir.dt.bfloat16
    ACT, ALU, AX = mybir.ActivationFunctionType, mybir.AluOpType, mybir.AxisListType
    IDENT = ACT.Identity

    with ExitStack() as ctx:
        def sb(name, shape, dt=f32):
            return ctx.enter_context(nc.sbuf_tensor(name, shape, dt))

        def ps(name, shape):
            return ctx.enter_context(nc.psum_tensor(name, shape, f32))

        def sem(name):
            return ctx.enter_context(nc.semaphore(name))

        first_sb = sb("first_sb", [128, 256 + HW + PARAMS])
        second_sb = sb("second_sb", [128, 256 + HW])
        third_sb = sb("third_sb", [128, 256])
        x_sb = [t[:, 256:256 + HW] for t in (first_sb, second_sb)]
        wqk_sb = [t[:, 0:256].rearrange("p (n o) -> p n o", n=2) for t in (first_sb, second_sb)]
        par_sb = first_sb[:, 256 + HW:256 + HW + PARAMS]
        wv_sb, id_sb = third_sb[:, 0:128], third_sb[:, 128:256]
        id_r = sb("id_r", [128, 128], f32r)
        junk = sb("junk", [128, Q], bf16)
        warm = sb("warm", [128, 1])
        q_hh = sb("q_hh", [128, CHUNKS, HW], f32r)
        q_lo = sb("q_lo", [128, CHUNKS, HW], f32r)
        q_ls = sb("q_ls", [128, CHUNKS, HW], f32r)
        k_tmp = sb("k_tmp", [128, CHUNKS, HW], f32r)
        k_hl = sb("k_hl", [128, CHUNKS, HW], f32r)
        k_h1 = sb("k_h1", [128, CHUNKS, HW], f32r)
        k_of = sb("k_of", [128, NH, HW], f32r)
        v_sb = sb("v_sb", [128, B * T, HEADS, 2 * D])
        rowmax = sb("rowmax", [128, CHUNKS, HPC, T])
        shift = sb("shift", [128, CHUNKS, T, HPC, Q], f32r)
        p_sb = sb("p_sb", [128, 2, HPC, T, HW])
        o_sb = sb("o_sb", [128, CHUNKS, HW])
        rden = sb("rden", [128, CHUNKS, T, HPC])
        o_t = sb("o_t", [128, B, T, HEADS, D])
        gbv = sb("gbv", [128, 1])
        xg = sb("xg", [C, B, HW])
        y_sb = sb("y_sb", [C, B, HW])

        banks = [ps(f"bank{n}", [128, 512]) for n in range(8)]
        s_ps = banks[0:SLOTS]
        e_ps = banks[SLOTS:2 * SLOTS]
        m_ps, o_ps = banks[6], banks[7]
        y_ps = [banks[b][:, 0:HW] for b in range(B)]
        q_ps = [banks[n][:, 0:HW] for n in (3, 5, 7, 4)]
        k_ps = [banks[n][:, 0:HW] for n in (4, 6, 3, 5)]
        v_ps = banks[7]

        in_first, in_second, in_third = (sem(n) for n in ("in_first", "in_second", "in_third"))
        junk_set, ones_set, shift_zeroed, id_rounded = (
            sem(n) for n in ("junk_set", "ones_set", "shift_zeroed", "id_rounded"))
        q_projected, k_projected, v_projected = (sem(n) for n in ("q_projected", "k_projected", "v_projected"))
        q_hh_ready, q_lo_ready, q_ls_ready = (sem(n) for n in ("q_hh_ready", "q_lo_ready", "q_ls_ready"))
        k_tmp_ready, k_hl_ready, k_h1_ready = (sem(n) for n in ("k_tmp_ready", "k_hl_ready", "k_h1_ready"))
        k_of_ready, v_ready, gbv_ready, xg_ready = (sem(n) for n in ("k_of_ready", "v_ready", "gbv_ready", "xg_ready"))
        scored, maxed, shift_ready, shift_placed = (
            sem(n) for n in ("scored", "maxed", "shift_ready", "shift_placed"))
        head_scored, head_exped, chunk_summed, sums_copied = (
            sem(n) for n in ("head_scored", "head_exped", "chunk_summed", "sums_copied"))
        sums_turned, rden_ready, o_t_ready, image_turned, y_ready = (
            sem(n) for n in ("sums_turned", "rden_ready", "o_t_ready", "image_turned", "y_ready"))
        stored = [sem(f"stored{b}") for b in range(B)]

        def rows(g):
            return slice(Q * g, Q * g + Q)

        out_d = out.rearrange("b c h w -> b c (h w)")
        block = ctx.enter_context(nc.Block())

        @block.sync
        def _(sp):
            sp.dma_start(first_sb[:], first).then_inc(in_first, 16)
            sp.dma_start(second_sb[:], second).then_inc(in_second, 16)
            sp.dma_start(third_sb[:], third).then_inc(in_third, 16)
            for b in range(B):
                sp.wait_ge(y_ready, b + 1)
                sp.dma_start(out_d[b], y_sb[:, b]).then_inc(stored[b], 16)
            for b in range(B):
                sp.wait_ge(stored[b], 16)

        @block.gpsimd
        def _(pool):
            nc.gpsimd.memset(shift[:].bitcast(f32), 0.0).then_inc(shift_zeroed, 1)
            nc.gpsimd.memset(v_sb[:, :, :, D:2 * D], 1.0).then_inc(ones_set, 1)
            pool.wait_ge(in_first, 16)
            nc.gpsimd.tensor_tensor(gbv[:], par_sb[:, BV:BV + 1], par_sb[:, GAMMA:GAMMA + 1],
                                    ALU.mult).then_inc(gbv_ready, 1)
            pool.wait_ge(in_third, 16)
            nc.gpsimd.tensor_copy(id_r[:], id_sb[:]).then_inc(id_rounded, 1)
            pool.wait_ge(shift_zeroed, 1)

            def isolate(c):
                pool.wait_ge(k_hl_ready, c + 1)
                for g in range(HPC):
                    nc.gpsimd.tensor_scalar(k_of[:, HPC * c + g], k_hl[:, c].bitcast(f32),
                                            par_sb[:, HEAD + g:HEAD + g + 1], 1.0, ALU.mult,
                                            ALU.mult).then_inc(k_of_ready, 1)

            def negate(c):
                pool.wait_ge(maxed, HPC * (c + 1))
                nc.gpsimd.tensor_scalar(shift[:, c, :, :, D:D + 1],
                                        rowmax[:, c].rearrange("p g (t o) -> p t g o", o=1), -1.0, 1.0,
                                        ALU.mult, ALU.mult).then_inc(shift_ready, 1)

            def residual(b):
                pool.wait_ge((in_first, in_second)[b], 16)
                nc.gpsimd.tensor_scalar(xg[:, b], x_sb[b], 1.0, gbv[:], ALU.mult, ALU.add).then_inc(xg_ready, 1)

            isolate(0)
            negate(0)
            pool.wait_ge(gbv_ready, 1)
            isolate(1)
            negate(1)
            isolate(2)
            residual(0)
            negate(2)
            isolate(3)
            residual(1)
            negate(3)

        @block.scalar
        def _(act):
            act.wait_ge(junk_set, 1)
            nc.scalar.activation(warm[:], junk[:, 0:1], ACT.Exp)
            act.wait_ge(in_first, 16)

            def col(n):
                return par_sb[:, n:n + 1]

            def round_queries(c):
                act.wait_ge(q_projected, c + 1)
                nc.scalar.activation(q_hh[:, c], q_ps[c], IDENT, bias=col(BQ + c % GROUPS)).then_inc(q_hh_ready, 1)

            def round_keys(c):
                act.wait_ge(k_projected, c + 1)
                nc.scalar.activation(k_tmp[:, c], k_ps[c], IDENT, bias=col(BK_LO + c % GROUPS),
                                     scale=col(IS_LO)).then_inc(k_tmp_ready, 1)

            def keys_and_ones(c):
                act.wait_ge(k_hl_ready, c + 1)
                nc.scalar.activation(k_h1[:, c], k_ps[c], IDENT, bias=col(BK_H1 + c % GROUPS),
                                     scale=col(IS_HI)).then_inc(k_h1_ready, 1)

            def exp(n):
                c, g = n // HPC, n % HPC
                act.wait_ge(head_scored, n + 1)
                if c >= 2:
                    act.wait_ge(chunk_summed, c - 1)
                nc.scalar.activation(p_sb[:, c % 2, g].rearrange("p t n -> p (t n)"), e_ps[n % SLOTS][:],
                                     ACT.Exp).then_inc(head_exped, 1)

            def copy_sums(c):
                act.wait_ge(chunk_summed, c + 1)
                nc.scalar.activation(o_sb[:, c], o_ps[:, 0:HW], ACT.Copy).then_inc(sums_copied, 1)

            for c in range(CHUNKS):
                round_keys(c)
                round_queries(c)
                keys_and_ones(c)
            act.wait_ge(v_projected, 1)
            act.wait_ge(ones_set, 1)
            nc.scalar.activation(v_sb[:, :, :, 0:D].rearrange("p t h d -> p (t h) d"),
                                 v_ps[:].rearrange("p (n d) -> p n d", d=D), ACT.Copy).then_inc(v_ready, 1)
            for n in range(NH):
                exp(n)
                if n > HPC and n % HPC == 2:
                    copy_sums(n // HPC - 1)
            copy_sums(CHUNKS - 1)

        @block.vector
        def _(dve):
            nc.vector.memset(junk[:], 0.5).then_inc(junk_set, 1)
            dve.wait_ge(in_first, 16)

            def col(n):
                return par_sb[:, n:n + 1]

            def split_keys(c):
                dve.wait_ge(k_tmp_ready, c + 1)
                nc.vector.scalar_tensor_tensor(out=k_hl[:, c], in0=k_ps[c], scalar=col(BK + c % GROUPS),
                                               in1=k_tmp[:, c].bitcast(f32), op0=ALU.add,
                                               op1=ALU.subtract).then_inc(k_hl_ready, 1)

            def split_queries(c):
                dve.wait_ge(q_hh_ready, c + 1)
                nc.vector.scalar_tensor_tensor(out=q_lo[:, c], in0=q_ps[c], scalar=col(BQ + c % GROUPS),
                                               in1=q_hh[:, c].bitcast(f32), op0=ALU.add,
                                               op1=ALU.subtract).then_inc(q_lo_ready, 1)

            def maximum(n):
                dve.wait_ge(scored, n + 1)
                nc.vector.tensor_reduce(rowmax[:, n // HPC, n % HPC], s_ps[n % SLOTS][:].rearrange("p (t n) -> p t n", t=T),
                                        axis=AX.X, op=ALU.max).then_inc(maxed, 1)

            def place(c):
                dve.wait_ge(shift_placed, c + 1)
                dve.wait_ge(q_lo_ready, c + 1)
                nc.vector.scalar_tensor_tensor(out=q_ls[:, c], in0=q_lo[:, c].bitcast(f32), scalar=col(IS_HI),
                                               in1=m_ps[:, 0:HW], op0=ALU.mult,
                                               op1=ALU.add).then_inc(q_ls_ready, 1)

            def normalise(c):
                b, g = c // GROUPS, c % GROUPS
                sums = m_ps[:, HW:2 * HW].rearrange("p (t g d) -> p t g d", t=T, d=Q)
                dve.wait_ge(sums_turned, c + 1)
                nc.vector.reciprocal(rden[:, c], sums[:, :, :, D]).then_inc(rden_ready, 1)
                dve.wait_ge(rden_ready, c + 1)
                for t in range(T):
                    last = nc.vector.tensor_tensor(o_t[:, b, t, HPC * g:HPC * g + HPC], sums[:, t, :, 0:D],
                                            rden[:, c, t].rearrange("p (g o) -> p g o", o=1).to_broadcast([128, HPC, D]), ALU.mult)
                last.then_inc(o_t_ready, 1)

            def residual(b):
                dve.wait_ge(image_turned, b + 1)
                dve.wait_ge(xg_ready, b + 1)
                nc.vector.scalar_tensor_tensor(out=y_sb[:, b], in0=y_ps[b], scalar=col(GAMMA),
                                               in1=xg[:, b], op0=ALU.mult, op1=ALU.add).then_inc(y_ready, 1)

            split_keys(0)
            split_queries(0)
            maximum(0)
            split_keys(1)
            maximum(1)
            maximum(2)
            split_queries(1)
            maximum(3)
            split_keys(2)
            place(0)
            split_keys(3)
            split_queries(2)
            split_queries(3)
            for n in range(HPC, NH):
                maximum(n)
                if n % HPC == 0 and n > HPC:
                    place(n // HPC - 1)
                if n == NH - 2:
                    normalise(0)
            place(CHUNKS - 1)
            normalise(1)
            residual(0)
            normalise(2)
            normalise(3)
            residual(1)

        @block.tensor
        def _(pe):
            def mm(o, lhsT, rhs, start=True, stop=True):
                return nc.tensor.matmul(o, lhsT, rhs, start=start, stop=stop)

            def project_keys(c):
                if c == 2:
                    pe.wait_ge(q_lo_ready, 1)
                if c == 3:
                    pe.wait_ge(q_lo_ready, 2)
                mm(k_ps[c], wqk_sb[c % GROUPS][:, 1], x_sb[c // GROUPS]).then_inc(k_projected, 1)

            def project_queries(c):
                if c == 3:
                    pe.wait_ge(k_h1_ready, 1)
                mm(q_ps[c], wqk_sb[c % GROUPS][:, 0], x_sb[c // GROUPS]).then_inc(q_projected, 1)

            def score(n):
                c, g = n // HPC, n % HPC
                if n >= SLOTS:
                    pe.wait_ge(maxed, n + 1 - SLOTS)
                if g == 0:
                    pe.wait_ge(q_hh_ready, c + 1)
                    pe.wait_ge(k_hl_ready, c + 1)
                for t in range(T):
                    last = mm(s_ps[n % SLOTS][:, HW * t:HW * t + HW], q_hh[rows(g), c, 128 * t:128 * t + 128],
                              k_hl[rows(g), c])
                last.then_inc(scored, 1)

            def turn_shift(c):
                pe.wait_ge(shift_ready, c + 1)
                if c == 0:
                    pe.wait_ge(k_h1_ready, 2)
                    pe.wait_ge(id_rounded, 1)
                if c >= 3:
                    pe.wait_ge(o_t_ready, c - 2)
                for t in range(T):
                    last = mm(m_ps[:, 128 * t:128 * t + 128], shift[:, c, t].rearrange("p g r -> p (g r)"),
                              id_r[:])
                last.then_inc(shift_placed, 1)

            def score_shifted(n):
                c, g = n // HPC, n % HPC
                if g == 0:
                    pe.wait_ge(q_ls_ready, c + 1)
                    pe.wait_ge(k_h1_ready, c + 1)
                if n == 0:
                    pe.wait_ge(k_h1_ready, 3)
                if n == 1:
                    pe.wait_ge(q_lo_ready, 4)
                if n == 2:
                    pe.wait_ge(k_h1_ready, 4)
                if n >= SLOTS:
                    pe.wait_ge(head_exped, n + 1 - SLOTS)
                pe.wait_ge(k_of_ready, n + 1)
                for t in range(T):
                    o = e_ps[n % SLOTS][:, HW * t:HW * t + HW]
                    keys = slice(128 * t, 128 * t + 128)
                    mm(o, k_of[:, n, keys], q_hh[:, c], stop=False)
                    last = mm(o, k_h1[rows(g), c, keys], q_ls[rows(g), c], start=False)
                last.then_inc(head_scored, 1)

            def weigh(c):
                b, group = c // GROUPS, c % GROUPS
                pe.wait_ge(head_exped, HPC * c + HPC)
                pe.wait_ge(v_ready, 1)
                if c:
                    pe.wait_ge(sums_copied, c)
                for t in range(T):
                    for g in range(HPC):
                        last = mm(o_ps[rows(g), 0:HW], v_sb[:, T * b + t, HPC * group + g],
                                  p_sb[:, c % 2, g, t], start=(t == 0), stop=(t == T - 1))
                last.then_inc(chunk_summed, 1)

            def turn_sums(c):
                pe.wait_ge(sums_copied, c + 1)
                if c:
                    pe.wait_ge(o_t_ready, c)
                pe.wait_ge(q_ls_ready, min(c + 3, CHUNKS))
                for t in range(T):
                    last = nc.tensor.transpose(m_ps[:, HW + 128 * t:HW + 128 * t + 128],
                                               o_sb[:, c, 128 * t:128 * t + 128], id_sb)
                last.then_inc(sums_turned, 1)

            def turn_image(b):
                pe.wait_ge(o_t_ready, GROUPS * (b + 1))
                pe.wait_ge(maxed, NH)
                for t in range(T):
                    last = nc.tensor.transpose(y_ps[b][:, 128 * t:128 * t + 128],
                                               o_t[:, b, t].rearrange("p h d -> p (h d)"), id_sb)
                last.then_inc(image_turned, 1)

            pe.wait_ge(junk_set, 1)
            for n in range(WARM):
                mm(banks[0][0:Q, :], junk[:], junk[:, 0:1].to_broadcast([128, 512]))
            pe.wait_ge(in_first, 16)
            project_keys(0)
            project_queries(0)
            pe.wait_ge(in_second, 16)
            project_keys(1)
            score(0)
            score(1)
            project_queries(1)
            score(2)
            project_keys(2)
            score(3)
            project_queries(2)
            score(4)
            project_keys(3)
            project_queries(3)
            score(5)
            turn_shift(0)
            pe.wait_ge(in_third, 16)
            pe.wait_ge(q_lo_ready, 3)
            for n in range(B * T):
                last = mm(v_ps[:, 128 * n:128 * n + 128], x_sb[n // T][:, 128 * (n % T):128 * (n % T) + 128],
                          wv_sb)
            last.then_inc(v_projected, 1)
            for n in range(NH):
                c, g = n // HPC, n % HPC
                if g == HPC - 1 and c + 1 < CHUNKS:
                    turn_shift(c + 1)
                score_shifted(n)
                if n + AHEAD < NH:
                    score(n + AHEAD)
                if c and g == 1:
                    weigh(c - 1)
                if c >= 2 and g == 0:
                    turn_sums(c - 2)
                if n == NH - 2:
                    turn_image(0)
            turn_sums(CHUNKS - 2)
            weigh(CHUNKS - 1)
            turn_sums(CHUNKS - 1)
            turn_image(B - 1)


def kernel(x, L0_conv_Wq, L0_conv_bq, L0_conv_Wk, L0_conv_bk, L0_conv_Wv, L0_conv_bv, L0_conv_gamma):
    import numpy as np
    import concourse.bacc as bacc
    from concourse.bass_utils import run_bass_kernel_spmd

    def twice(a):
        a = np.asarray(a)
        a = a.reshape(a.shape[:-1] + (GROUPS, HPC, 1, D))
        return np.ascontiguousarray(np.broadcast_to(a, a.shape[:-2] + (2, D))).reshape(a.shape[:-4] + (GROUPS, 128))

    upper = (np.arange(128) % Q) < D
    par = np.zeros((128, PARAMS), np.float32)
    for g in range(GROUPS):
        par[:, BQ + g] = twice(L0_conv_bq)[g]
        par[:, BK + g] = twice(L0_conv_bk)[g]
        par[~upper, BK_LO + g] = twice(L0_conv_bk)[g][~upper]
        par[upper, BK_H1 + g] = twice(L0_conv_bk)[g][upper]
        par[~upper, BK_H1 + g] = 1.0
    par[~upper, IS_LO] = 1.0
    par[upper, IS_HI] = 1.0
    par[:, BV] = np.asarray(L0_conv_bv)
    par[:, GAMMA] = np.asarray(L0_conv_gamma)[0]
    par[np.arange(128), HEAD + np.arange(128) // Q] = 1.0
    wq_t, wk_t = twice(np.asarray(L0_conv_Wq).T), twice(np.asarray(L0_conv_Wk).T)
    x = np.asarray(x)
    image = [x[b].reshape(C, HW) for b in range(B)]
    arrays = {
        "first_dram": np.concatenate([wq_t[:, 0], wk_t[:, 0], image[0], par], axis=1),
        "second_dram": np.concatenate([wq_t[:, 1], wk_t[:, 1], image[1]], axis=1),
        "third_dram": np.concatenate([np.asarray(L0_conv_Wv).T, np.eye(128, dtype=np.float32)], axis=1),
    }
    nc = bacc.Bacc("TRN2", target_bir_lowering=False, num_devices=1)
    f32 = mybir.dt.float32
    args = [nc.dram_tensor(n, a.shape, f32, kind="ExternalInput").ap() for n, a in arrays.items()]
    out = nc.dram_tensor("out_dram", (B, C, 16, 16), f32, kind="ExternalOutput").ap()
    build(nc, *args, out)
    return run_bass_kernel_spmd(nc, [arrays], core_ids=[0]).results[0]["out_dram"]
```

```python
import concourse.bass as bass
from concourse import mybir
from contextlib import ExitStack

B, C, HW = 2, 128, 256
HEADS, D = 8, 16
Q = 32
HPC = 128 // Q
GROUPS = HEADS // HPC
CHUNKS = B * GROUPS
NH = HPC * CHUNKS
T = HW // 128
SLOTS = 3
WARM = 6
LAST = CHUNKS - 1
DVE_CUTS = (0, 3)

BQ, BK, BK_LO, BK_H1, IS_LO, IS_HI, BV, GAMMA, HEAD, PAIR = 0, 2, 4, 6, 8, 9, 10, 11, 12, 16
PARAMS = 18


def build(nc, keys_in, queries_in, second, third, out):
    f32, f32r, bf16 = mybir.dt.float32, mybir.dt.float32r, mybir.dt.bfloat16
    ACT, ALU, AX = mybir.ActivationFunctionType, mybir.AluOpType, mybir.AxisListType
    IDENT = ACT.Identity

    with ExitStack() as ctx:
        def sb(name, shape, dt=f32):
            return ctx.enter_context(nc.sbuf_tensor(name, shape, dt))

        def ps(name, shape):
            return ctx.enter_context(nc.psum_tensor(name, shape, f32))

        def sem(name):
            return ctx.enter_context(nc.semaphore(name))

        keys_in_sb = sb("keys_in_sb", [128, 128 + HW])
        queries_in_sb = sb("queries_in_sb", [128, 128 + PARAMS])
        second_sb = sb("second_sb", [128, 256 + HW])
        third_sb = sb("third_sb", [128, 384])
        x_sb = [keys_in_sb[:, 128:128 + HW], second_sb[:, 256:256 + HW]]
        wk_sb = [keys_in_sb[:, 0:128], second_sb[:, 128:256]]
        wq_sb = [queries_in_sb[:, 0:128], second_sb[:, 0:128]]
        par_sb = queries_in_sb[:, 128:128 + PARAMS]
        wv_sb, id_sb = third_sb[:, 0:128], third_sb[:, 128:256]
        turn_r = sb("turn_r", [128, 4, 128], f32r)
        turns = [turn_r[:, 1 - t:3 - t].rearrange("p a b -> p (a b)") for t in range(T)]
        swap_r = turn_r[:, 3]
        table_warm = sb("table_warm", [128, 1])
        q_hh = sb("q_hh", [128, HW], f32r)
        q_f = sb("q_f", [128, CHUNKS, HW])
        q_lo = sb("q_lo", [128, CHUNKS, HW], f32r)
        q_ls = sb("q_ls", [128, HW], f32r)
        q_cat = sb("q_cat", [128, CHUNKS, 2, HW], f32r)
        k_tmp = sb("k_tmp", [128, CHUNKS, HW], f32r)
        k_hl = sb("k_hl", [128, HW], f32r)
        k_h1 = sb("k_h1", [128, CHUNKS, HW], f32r)
        k_cat = sb("k_cat", [128, CHUNKS, 2, HW], f32r)
        k_of = sb("k_of", [128, NH, HW], f32r)
        v_sb = sb("v_sb", [128, B * T, HEADS, 2 * D])
        shift = sb("shift", [128, LAST, T, HPC, Q], f32r)
        shift_last = sb("shift_last", [128, T, HPC + 2, Q], f32r)
        p_sb = sb("p_sb", [128, CHUNKS, HPC, T, HW])
        o_sb = sb("o_sb", [128, CHUNKS, HW])
        rden = sb("rden", [128, CHUNKS, T, HPC])
        o_t = sb("o_t", [128, B, T, HEADS, D])
        gbv = sb("gbv", [128, 1])
        xg = sb("xg", [C, B, HW])
        y_sb = sb("y_sb", [C, B, HW])

        banks = [ps(f"bank{n}", [128, 512]) for n in range(8)]
        s_ps = banks[0:SLOTS]
        e_ps = [banks[5], banks[3], banks[4]]
        placed_ps, turned_ps = banks[6][:, 0:HW], banks[6][:, HW:2 * HW]
        o_ps = banks[7][:, 0:HW]
        y0_ps = banks[0][:, 0:HW]
        last_sums = [banks[3][:, 0:128], banks[4][:, 0:128]]
        last_turned = [banks[5][:, 0:128], banks[7][:, 0:128]]
        last_y = [banks[1][:, 0:128], banks[2][:, 0:128]]
        q_ps = [banks[3][:, 0:HW], banks[5][:, 0:HW], banks[4][:, 0:HW], banks[7][:, HW:2 * HW]]
        k_ps = [banks[4][:, 0:HW], banks[7][:, 0:HW], banks[3][:, 0:HW], banks[7][:, 0:HW]]
        v_ps = banks[6]

        keys_came, queries_came, second_came, third_came = (
            sem(n) for n in ("keys_came", "queries_came", "second_came", "third_came"))
        ones_set, shift_zeroed, turns_zeroed, turns_rounded = (
            sem(n) for n in ("ones_set", "shift_zeroed", "turns_zeroed", "turns_rounded"))
        q_projected, k_projected, v_projected = (
            sem(n) for n in ("q_projected", "k_projected", "v_projected"))
        q_hh_ready, q_f_ready, q_lo_ready = (
            [sem(f"{n}{c}") for c in range(CHUNKS)] for n in ("q_hh_ready", "q_f_ready", "q_lo_ready"))
        k_tmp_ready, k_hl_ready, k_h1_ready, k_of_ready, v_ready = (
            sem(n) for n in ("k_tmp_ready", "k_hl_ready", "k_h1_ready", "k_of_ready", "v_ready"))
        q_copied, k_copied = ([sem(f"{n}{c}") for c in range(CHUNKS)] for n in ("q_copied", "k_copied"))
        k_carried = [[sem(f"k_carried{c}_{h}") for h in range(2)] for c in range(CHUNKS)]
        scored, maxed, shift_turned, shift_placed = (
            sem(n) for n in ("scored", "maxed", "shift_turned", "shift_placed"))
        head_scored, head_exped, chunk_summed, sums_copied = (
            sem(n) for n in ("head_scored", "head_exped", "chunk_summed", "sums_copied"))
        sums_turned, rden_ready, o_t_ready, image_turned, y_ready = (
            sem(n) for n in ("sums_turned", "rden_ready", "o_t_ready", "image_turned", "y_ready"))
        gbv_ready, xg_ready = (sem(n) for n in ("gbv_ready", "xg_ready"))
        stored = [sem(f"stored{b}") for b in range(B)]

        def rows(g):
            return slice(Q * g, Q * g + Q)

        def half(h):
            return slice(64 * h, 64 * h + 64)

        def q_hh_of(c):
            return q_cat[:, c, 0] if c else q_hh[:]

        def k_hl_of(c):
            return k_cat[:, c, 0] if c else k_hl[:]

        def tile(t):
            return slice(128 * t, 128 * t + 128)

        def halves(c, h):
            return 2 * c + h if c else 1

        out_d = out.rearrange("b c h w -> b c (h w)")
        block = ctx.enter_context(nc.Block())

        @block.sync
        def _(sp):
            sp.dma_start(keys_in_sb[:], keys_in).then_inc(keys_came, 16)
            sp.dma_start(queries_in_sb[:], queries_in).then_inc(queries_came, 16)
            sp.dma_start(second_sb[:], second).then_inc(second_came, 16)
            sp.dma_start(third_sb[:], third).then_inc(third_came, 16)

            def carry_keys(c, h):
                sp.wait_ge(k_h1_ready, c + 1)
                sp.wait_ge(k_copied[c], 1)
                sp.dma_start(k_cat[half(1 - h), c, h].bitcast(f32),
                             k_h1[half(h), c].bitcast(f32)).then_inc(k_carried[c][h], 16)

            carry_keys(1, 0)
            carry_keys(1, 1)
            carry_keys(2, 0)
            carry_keys(2, 1)
            carry_keys(3, 0)
            carry_keys(3, 1)
            sp.wait_ge(y_ready, 1)
            sp.dma_start(out_d[0], y_sb[:, 0]).then_inc(stored[0], 16)
            sp.wait_ge(y_ready, 1 + T)
            sp.dma_start(out_d[1], y_sb[:, 1]).then_inc(stored[1], 16)
            for b in range(B):
                sp.wait_ge(stored[b], 16)

        @block.gpsimd
        def _(pool):
            nc.gpsimd.memset(shift[:].bitcast(f32), 0.0).then_inc(shift_zeroed, 1)
            nc.gpsimd.memset(shift_last[:].bitcast(f32), 0.0).then_inc(shift_zeroed, 1)
            nc.gpsimd.memset(turn_r[:, 0::2].bitcast(f32), 0.0).then_inc(turns_zeroed, 1)
            nc.gpsimd.memset(v_sb[:, :, :, D:2 * D], 1.0).then_inc(ones_set, 1)
            pool.wait_ge(queries_came, 16)
            nc.gpsimd.tensor_tensor(gbv[:], par_sb[:, BV:BV + 1], par_sb[:, GAMMA:GAMMA + 1],
                                    ALU.mult).then_inc(gbv_ready, 1)
            pool.wait_ge(third_came, 16)
            nc.gpsimd.tensor_copy(turn_r[:, 1::2], third_sb[:, 128:384].rearrange("p (a b) -> p a b", b=128)
                                  ).then_inc(turns_rounded, 1)

            def isolate(n):
                c, g = n // HPC, n % HPC
                if c == 0:
                    pool.wait_ge(k_hl_ready, 1)
                    source, mask = k_hl[:], par_sb[:, HEAD + g:HEAD + g + 1]
                else:
                    pool.wait_ge(k_carried[c][g // 2], 16)
                    pool.wait_ge(k_copied[c], 1)
                    source, mask = k_cat[:, c, g // 2], par_sb[:, PAIR + g % 2:PAIR + g % 2 + 1]
                nc.gpsimd.tensor_scalar(k_of[:, n], source.bitcast(f32), mask, 1.0, ALU.mult,
                                        ALU.mult).then_inc(k_of_ready, 1)

            def cut_queries(c):
                pool.wait_ge(q_hh_ready[c], 1)
                pool.wait_ge(q_f_ready[c], 1)
                nc.gpsimd.tensor_tensor(q_lo[:, c], q_f[:, c], q_hh_of(c).bitcast(f32),
                                        ALU.subtract).then_inc(q_lo_ready[c], 1)

            def copy_keys(c):
                pool.wait_ge(k_hl_ready, c + 1)
                nc.gpsimd.tensor_copy(k_cat[:, c, 1], k_cat[:, c, 0].bitcast(f32)).then_inc(k_copied[c], 1)

            def copy_queries(c):
                pool.wait_ge(q_hh_ready[c], 1)
                nc.gpsimd.tensor_copy(q_cat[:, c, 1], q_cat[:, c, 0].bitcast(f32)).then_inc(q_copied[c], 1)

            def residual_base(b):
                pool.wait_ge((keys_came, second_came)[b], 16)
                pool.wait_ge(gbv_ready, 1)
                nc.gpsimd.tensor_scalar(xg[:, b], x_sb[b], 1.0, gbv[:], ALU.mult, ALU.add).then_inc(xg_ready, 1)

            for n in range(4):
                isolate(n)
            copy_keys(1)
            copy_queries(1)
            cut_queries(1)
            copy_keys(2)
            cut_queries(2)
            copy_queries(3)
            for n in range(4, 9):
                isolate(n)
            residual_base(0)
            for n in range(9, 14):
                isolate(n)
            residual_base(1)
            isolate(14)
            isolate(15)

        @block.scalar
        def _(act):
            nc.scalar.activation(table_warm[:], nc.const_aps.tensor(1.0, [128, 1], f32), ACT.Exp)
            act.wait_ge(queries_came, 16)

            def col(n):
                return par_sb[:, n:n + 1]

            def round_queries(c):
                act.wait_ge(q_projected, c + 1)
                nc.scalar.activation(q_hh_of(c), q_ps[c], IDENT,
                                     bias=col(BQ + c % GROUPS)).then_inc(q_hh_ready[c], 1)

            def keep_queries(c):
                act.wait_ge(q_projected, c + 1)
                nc.scalar.activation(q_f[:, c], q_ps[c], IDENT,
                                     bias=col(BQ + c % GROUPS)).then_inc(q_f_ready[c], 1)

            def round_keys(c):
                act.wait_ge(k_projected, c + 1)
                nc.scalar.activation(k_tmp[:, c], k_ps[c], IDENT, bias=col(BK_LO + c % GROUPS),
                                     scale=col(IS_LO)).then_inc(k_tmp_ready, 1)

            def keys_and_ones(c, after_split=False):
                act.wait_ge(k_projected, c + 1)
                if after_split:
                    act.wait_ge(k_hl_ready, c + 1)
                nc.scalar.activation(k_h1[:, c], k_ps[c], IDENT, bias=col(BK_H1 + c % GROUPS),
                                     scale=col(IS_HI)).then_inc(k_h1_ready, 1)

            def copy_values():
                act.wait_ge(v_projected, 1)
                nc.scalar.activation(v_sb[:, :, :, 0:D].rearrange("p t h d -> p (t h) d"),
                                     v_ps[:].rearrange("p (n d) -> p n d", d=D), ACT.Copy).then_inc(v_ready, 1)

            def place_shift(c, h):
                act.wait_ge(shift_turned, halves(c, h))
                act.wait_ge(q_copied[c], 1)
                nc.scalar.activation(q_cat[half(1 - h), c, h], placed_ps[half(1 - h)],
                                     ACT.Copy).then_inc(shift_placed, 1)

            def exp(n):
                c, g = n // HPC, n % HPC
                act.wait_ge(head_scored, n + 1)
                if n < NH - 1:
                    nc.scalar.activation(p_sb[:, c, g].rearrange("p t n -> p (t n)"), e_ps[n % SLOTS][:],
                                         ACT.Exp).then_inc(head_exped, 1)
                else:
                    for t in range(T):
                        nc.scalar.activation(p_sb[:, c, g, t], e_ps[n % SLOTS][:, HW * t:HW * t + HW],
                                             ACT.Exp).then_inc(head_exped, 1)

            def copy_sums(c):
                act.wait_ge(chunk_summed, c + 1)
                nc.scalar.activation(o_sb[:, c], o_ps, ACT.Copy).then_inc(sums_copied, 1)

            keys_and_ones(0)
            round_queries(0)
            round_keys(0)
            keys_and_ones(1)
            round_keys(1)
            round_queries(1)
            keep_queries(1)
            round_queries(2)
            round_keys(2)
            round_keys(3)
            copy_values()
            keys_and_ones(2, after_split=True)
            keys_and_ones(3, after_split=True)
            keep_queries(2)
            round_queries(3)
            exp(0)
            exp(1)
            place_shift(1, 0)
            place_shift(1, 1)
            for n in range(2, 7):
                exp(n)
            place_shift(2, 0)
            place_shift(2, 1)
            exp(7)
            copy_sums(0)
            for n in range(8, 12):
                exp(n)
            copy_sums(1)
            exp(12)
            exp(13)
            copy_sums(2)
            exp(14)
            exp(15)
            for t in range(T):
                act.wait_ge(chunk_summed, CHUNKS + t)
                nc.scalar.activation(o_sb[:, LAST, tile(t)], last_sums[t], ACT.Copy).then_inc(sums_copied, 1)

        @block.vector
        def _(dve):
            dve.wait_ge(queries_came, 16)

            def col(n):
                return par_sb[:, n:n + 1]

            def split_keys(c):
                dve.wait_ge(k_tmp_ready, c + 1)
                nc.vector.scalar_tensor_tensor(out=k_hl_of(c), in0=k_ps[c], scalar=col(BK + c % GROUPS),
                                               in1=k_tmp[:, c].bitcast(f32), op0=ALU.add,
                                               op1=ALU.subtract).then_inc(k_hl_ready, 1)

            def cut_queries(c):
                dve.wait_ge(q_hh_ready[c], 1)
                nc.vector.scalar_tensor_tensor(out=q_lo[:, c], in0=q_ps[c], scalar=col(BQ + c % GROUPS),
                                               in1=q_hh_of(c).bitcast(f32), op0=ALU.add,
                                               op1=ALU.subtract).then_inc(q_lo_ready[c], 1)

            def copy_keys(c):
                dve.wait_ge(k_hl_ready, c + 1)
                nc.vector.tensor_copy(k_cat[:, c, 1], k_cat[:, c, 0].bitcast(f32)).then_inc(k_copied[c], 1)

            def copy_queries(c):
                dve.wait_ge(q_hh_ready[c], 1)
                nc.vector.tensor_copy(q_cat[:, c, 1], q_cat[:, c, 0].bitcast(f32)).then_inc(q_copied[c], 1)

            def maximum(n):
                c, g = n // HPC, n % HPC
                dve.wait_ge(scored, n + 1)
                if n == 0:
                    dve.wait_ge(shift_zeroed, 2)
                if c == 0:
                    column = shift[:, 0, :, g, D]
                elif c < LAST:
                    column = shift[:, c, :, g ^ 2, D]
                else:
                    column = shift_last[:, :, g + 4 if g < 2 else g - 2, D]
                nc.vector.tensor_reduce(column, s_ps[n % SLOTS][:].rearrange("p (t n) -> p t n", t=T),
                                        axis=AX.X, op=ALU.max, negate=True).then_inc(maxed, 1)

            def place_shift(c, h=0):
                dve.wait_ge(shift_turned, halves(c, h))
                if c == 0:
                    dve.wait_ge(q_lo_ready[0], 1)
                    nc.vector.scalar_tensor_tensor(out=q_ls[:], in0=q_lo[:, 0].bitcast(f32), scalar=col(IS_HI),
                                                   in1=placed_ps, op0=ALU.mult,
                                                   op1=ALU.add).then_inc(shift_placed, 1)
                else:
                    dve.wait_ge(q_copied[c], 1)
                    nc.vector.tensor_copy(q_cat[half(1 - h), c, h],
                                          placed_ps[half(1 - h)]).then_inc(shift_placed, 1)

            def normalise(c):
                b, g = c // GROUPS, c % GROUPS
                sums = turned_ps.rearrange("p (t g d) -> p t g d", t=T, d=Q)
                dve.wait_ge(sums_turned, c + 1)
                nc.vector.reciprocal(rden[:, c], sums[:, :, :, D]).then_inc(rden_ready, 1)
                dve.wait_ge(rden_ready, c + 1)
                nc.vector.tensor_tensor(
                    o_t[:, b, :, HPC * g:HPC * g + HPC], sums[:, :, :, 0:D],
                    rden[:, c].rearrange("p t (g o) -> p t g o", o=1).to_broadcast([128, T, HPC, D]),
                    ALU.mult).then_inc(o_t_ready, 1)

            def normalise_last(t):
                sums = last_turned[t].rearrange("p (g d) -> p g d", d=Q)
                dve.wait_ge(sums_turned, CHUNKS + t)
                nc.vector.reciprocal(rden[:, LAST, t], sums[:, :, D]).then_inc(rden_ready, 1)
                dve.wait_ge(rden_ready, CHUNKS + t)
                nc.vector.tensor_tensor(
                    o_t[:, B - 1, t, HEADS - HPC:HEADS], sums[:, :, 0:D],
                    rden[:, LAST, t].rearrange("p (g o) -> p g o", o=1).to_broadcast([128, HPC, D]),
                    ALU.mult).then_inc(o_t_ready, 1)

            def residual_first():
                dve.wait_ge(image_turned, 1)
                dve.wait_ge(xg_ready, 1)
                nc.vector.scalar_tensor_tensor(out=y_sb[:, 0], in0=y0_ps, scalar=col(GAMMA), in1=xg[:, 0],
                                               op0=ALU.mult, op1=ALU.add).then_inc(y_ready, 1)

            def residual_last(t):
                dve.wait_ge(image_turned, B + t)
                dve.wait_ge(xg_ready, B)
                nc.vector.scalar_tensor_tensor(out=y_sb[:, B - 1, tile(t)], in0=last_y[t], scalar=col(GAMMA),
                                               in1=xg[:, B - 1, tile(t)], op0=ALU.mult,
                                               op1=ALU.add).then_inc(y_ready, 1)

            cut_queries(0)
            split_keys(0)
            maximum(0)
            split_keys(1)
            for n in range(1, 4):
                maximum(n)
            split_keys(2)
            split_keys(3)
            maximum(4)
            place_shift(0)
            for n in range(5, 8):
                maximum(n)
            copy_queries(2)
            for n in range(8, 12):
                maximum(n)
            copy_keys(3)
            cut_queries(3)
            for n in range(12, 16):
                maximum(n)
            place_shift(3, 0)
            place_shift(3, 1)
            normalise(0)
            normalise(1)
            normalise(2)
            residual_first()
            for t in range(T):
                normalise_last(t)
            for t in range(T):
                residual_last(t)

        @block.tensor
        def _(pe):
            def mm(o, lhsT, rhs, start=True, stop=True):
                return nc.tensor.matmul(o, lhsT, rhs, start=start, stop=stop)

            def wait_queries_read(c):
                pe.wait_ge(q_hh_ready[c], 1)
                pe.wait_ge(q_lo_ready[c] if c in DVE_CUTS else q_f_ready[c], 1)

            def wait_keys_read(c):
                pe.wait_ge(k_h1_ready, c + 1)
                pe.wait_ge(k_hl_ready, c + 1)

            def project_keys(c):
                if c == 0:
                    pe.wait_ge(keys_came, 16)
                if c == 1:
                    pe.wait_ge(second_came, 16)
                if c == 2:
                    wait_queries_read(0)
                if c == 3:
                    wait_keys_read(1)
                mm(k_ps[c], wk_sb[c % GROUPS], x_sb[c // GROUPS]).then_inc(k_projected, 1)

            def project_queries(c):
                if c == 0:
                    pe.wait_ge(keys_came, 16)
                    pe.wait_ge(queries_came, 16)
                if c == 1:
                    pe.wait_ge(second_came, 16)
                if c == 2:
                    wait_keys_read(0)
                if c == 3:
                    wait_keys_read(3)
                mm(q_ps[c], wq_sb[c % GROUPS], x_sb[c // GROUPS]).then_inc(q_projected, 1)

            def project_values():
                pe.wait_ge(second_came, 16)
                pe.wait_ge(third_came, 16)
                for n in range(B * T):
                    last = mm(v_ps[:, tile(n)], x_sb[n // T][:, tile(n % T)], wv_sb)
                last.then_inc(v_projected, 1)

            def score(n):
                c, g = n // HPC, n % HPC
                if n >= SLOTS:
                    pe.wait_ge(maxed, n + 1 - SLOTS)
                if g == 0:
                    pe.wait_ge(q_hh_ready[c], 1)
                    pe.wait_ge(k_hl_ready if c else k_h1_ready, c + 1)
                if c and g == 2:
                    pe.wait_ge(q_copied[c], 1)
                    pe.wait_ge(k_copied[c], 1)
                upper = slice(Q * g, Q * g + D)
                for t in range(T):
                    o = s_ps[n % SLOTS][:, HW * t:HW * t + HW]
                    if c == 0:
                        last = mm(o, q_hh[upper, tile(t)], k_h1[upper, 0])
                    else:
                        last = mm(o, q_cat[rows(g), c, g // 2, tile(t)], k_cat[rows(g), c, g // 2])
                last.then_inc(scored, 1)

            def turn_shift(c, sums_read=0):
                if sums_read:
                    pe.wait_ge(o_t_ready, sums_read)
                pe.wait_ge(maxed, HPC * (c + 1))
                if c == 0:
                    pe.wait_ge(v_ready, 1)
                    pe.wait_ge(turns_rounded, 1)
                    pe.wait_ge(turns_zeroed, 1)
                else:
                    pe.wait_ge(shift_placed, halves(c - 1, 1))
                    pe.wait_ge(q_lo_ready[c], 1)
                    mm(placed_ps, swap_r, q_lo[:, c], stop=False)
                for t in range(T):
                    last = mm(placed_ps, shift[:, c, t].rearrange("p g r -> p (g r)"), turns[t],
                              start=(c == 0 and t == 0), stop=(t == T - 1))
                last.then_inc(shift_turned, 2 if c else 1)

            def turn_last_shift(h, sums_read=0):
                if sums_read:
                    pe.wait_ge(o_t_ready, sums_read)
                pe.wait_ge(maxed, HPC * LAST + 2 * h + 2)
                pe.wait_ge(shift_placed, halves(LAST - 1, 1))
                pe.wait_ge(q_lo_ready[LAST], 1)
                written, quadrants = (slice(0, 64), slice(0, 2)) if h else (slice(0, 128), slice(2, 6))
                mm(placed_ps[written], swap_r[:, written], q_lo[:, LAST], stop=False)
                for t in range(T):
                    last = mm(placed_ps[written], shift_last[:, t, quadrants].rearrange("p g r -> p (g r)"),
                              turns[t], start=False, stop=(t == T - 1))
                last.then_inc(shift_turned, 1)

            def begin_shifted(n):
                if n == 0:
                    wait_queries_read(1)
                if n == 1:
                    wait_keys_read(2)
                if n == 2:
                    wait_queries_read(2)
                if n >= SLOTS:
                    pe.wait_ge(head_exped, n + 1 - SLOTS)
                pe.wait_ge(k_of_ready, n + 1)
                mm(e_ps[n % SLOTS][:, 0:HW], k_of[:, n, tile(0)], q_hh[:], stop=False)

            def finish_shifted(n):
                if n == 0:
                    pe.wait_ge(shift_placed, halves(0, 0))
                for t in range(T):
                    o = e_ps[n % SLOTS][:, HW * t:HW * t + HW]
                    if t:
                        mm(o, k_of[:, n, tile(t)], q_hh[:], stop=False)
                    last = mm(o, k_h1[rows(n), 0, tile(t)], q_ls[rows(n)], start=False)
                last.then_inc(head_scored, 1)

            def score_shifted(n):
                c, g = n // HPC, n % HPC
                if g % 2 == 0:
                    pe.wait_ge(shift_placed, halves(c, g // 2))
                pe.wait_ge(head_exped, n + 1 - SLOTS)
                pe.wait_ge(k_of_ready, n + 1)
                for t in range(T):
                    last = mm(e_ps[n % SLOTS][:, HW * t:HW * t + HW], k_of[:, n, tile(t)], q_cat[:, c, g // 2])
                last.then_inc(head_scored, 1)

            def weigh(c):
                pe.wait_ge(head_exped, HPC * c + HPC)
                if c == 0:
                    pe.wait_ge(ones_set, 1)
                    wait_queries_read(3)
                else:
                    pe.wait_ge(sums_copied, c)
                for t in range(T):
                    for g in range(HPC):
                        last = mm(o_ps[rows(g)], v_sb[:, T * (c // GROUPS) + t, HPC * (c % GROUPS) + g],
                                  p_sb[:, c, g, t], start=(t == 0), stop=(t == T - 1))
                last.then_inc(chunk_summed, 1)

            def turn_sums(c, placed):
                pe.wait_ge(sums_copied, c + 1)
                if c:
                    pe.wait_ge(o_t_ready, c)
                pe.wait_ge(shift_placed, placed)
                for t in range(T):
                    last = nc.tensor.transpose(turned_ps[:, tile(t)], o_sb[:, c, tile(t)], id_sb)
                last.then_inc(sums_turned, 1)

            def turn_image():
                pe.wait_ge(o_t_ready, GROUPS)
                pe.wait_ge(maxed, NH)
                for t in range(T):
                    last = nc.tensor.transpose(y0_ps[:, tile(t)], o_t[:, 0, t].rearrange("p h d -> p (h d)"), id_sb)
                last.then_inc(image_turned, 1)

            for n in range(WARM):
                mm(banks[0][0:Q, :], nc.const_aps.tensor(1.0, [128, Q], bf16),
                   nc.const_aps.tensor(1.0, [128, 512], bf16))
            project_keys(0)
            project_queries(0)
            project_keys(1)
            project_queries(1)
            score(0)
            project_keys(2)
            score(1)
            project_queries(2)
            score(2)
            score(3)
            project_keys(3)
            project_values()
            begin_shifted(0)
            score(4)
            turn_shift(0)
            score(5)
            score(6)
            project_queries(3)
            finish_shifted(0)
            score(7)
            begin_shifted(1)
            finish_shifted(1)
            score(8)
            begin_shifted(2)
            score(9)
            begin_shifted(3)
            turn_shift(1)
            score(10)
            finish_shifted(2)
            finish_shifted(3)
            score(11)
            score_shifted(4)
            score(12)
            score_shifted(5)
            score(13)
            score_shifted(6)
            turn_shift(2)
            score(14)
            score_shifted(7)
            weigh(0)
            score(15)
            for n in range(8, 11):
                score_shifted(n)
            turn_last_shift(0)
            turn_last_shift(1)
            score_shifted(11)
            weigh(1)
            turn_sums(0, placed=halves(3, 1))
            score_shifted(12)
            score_shifted(13)
            weigh(2)
            turn_sums(1, placed=halves(3, 1))
            score_shifted(14)
            score_shifted(15)
            turn_sums(2, placed=halves(3, 1))
            turn_image()
            for kt in range(T):
                pe.wait_ge(head_exped, NH + kt)
                for qt in range(T):
                    for g in range(HPC):
                        last = mm(last_sums[qt][rows(g)], v_sb[:, T * (B - 1) + kt, HEADS - HPC + g],
                                  p_sb[:, LAST, g, kt, tile(qt)], start=(kt == 0), stop=(kt == T - 1))
                    if kt == T - 1:
                        last.then_inc(chunk_summed, 1)
            for t in range(T):
                pe.wait_ge(sums_copied, CHUNKS + t)
                nc.tensor.transpose(last_turned[t], o_sb[:, LAST, tile(t)], id_sb).then_inc(sums_turned, 1)
            for t in range(T):
                pe.wait_ge(o_t_ready, CHUNKS + t)
                nc.tensor.transpose(last_y[t], o_t[:, B - 1, t].rearrange("p h d -> p (h d)"),
                                    id_sb).then_inc(image_turned, 1)


def kernel(x, L0_conv_Wq, L0_conv_bq, L0_conv_Wk, L0_conv_bk, L0_conv_Wv, L0_conv_bv, L0_conv_gamma):
    import numpy as np
    import concourse.bacc as bacc
    from concourse.bass_utils import run_bass_kernel_spmd

    def twice(a):
        a = np.asarray(a)
        a = a.reshape(a.shape[:-1] + (GROUPS, HPC, 1, D))
        return np.ascontiguousarray(np.broadcast_to(a, a.shape[:-2] + (2, D))).reshape(a.shape[:-4] + (GROUPS, 128))

    row = np.arange(128)
    upper = row % Q < D
    par = np.zeros((128, PARAMS), np.float32)
    for g in range(GROUPS):
        par[:, BQ + g] = twice(L0_conv_bq)[g]
        par[:, BK + g] = twice(L0_conv_bk)[g]
        par[~upper, BK_LO + g] = twice(L0_conv_bk)[g][~upper]
        par[upper, BK_H1 + g] = twice(L0_conv_bk)[g][upper]
        par[~upper, BK_H1 + g] = 1.0
    par[~upper, IS_LO] = 1.0
    par[upper, IS_HI] = 1.0
    par[:, BV] = np.asarray(L0_conv_bv)
    par[:, GAMMA] = np.asarray(L0_conv_gamma)[0]
    par[row, HEAD + row // Q] = 1.0
    par[row, PAIR + row // Q % 2] = 1.0
    identity = np.eye(128, dtype=np.float32)
    swap = np.roll(identity, 64, axis=1)
    swap[~upper] = 0.0
    wq_t, wk_t = twice(np.asarray(L0_conv_Wq).T), twice(np.asarray(L0_conv_Wk).T)
    image = [np.asarray(x)[b].reshape(C, HW) for b in range(B)]
    arrays = {
        "keys_in_dram": np.concatenate([wk_t[:, 0], image[0]], axis=1),
        "queries_in_dram": np.concatenate([wq_t[:, 0], par], axis=1),
        "second_dram": np.concatenate([wq_t[:, 1], wk_t[:, 1], image[1]], axis=1),
        "third_dram": np.concatenate([np.asarray(L0_conv_Wv).T, identity, swap], axis=1),
    }
    nc = bacc.Bacc("TRN2", target_bir_lowering=False, num_devices=1)
    f32 = mybir.dt.float32
    args = [nc.dram_tensor(n, a.shape, f32, kind="ExternalInput").ap() for n, a in arrays.items()]
    out = nc.dram_tensor("out_dram", (B, C, 16, 16), f32, kind="ExternalOutput").ap()
    build(nc, *args, out)
    return run_bass_kernel_spmd(nc, [arrays], core_ids=[0]).results[0]["out_dram"]
```
